# Optimizing a Trainium2 kernel written in Bass

```python
import numpy as np
import jax
import jax.numpy as jnp

def _softmax(x, axis=-1):
    return jax.nn.softmax(x, axis=axis)
def _gelu(x):
    return jax.nn.gelu(x, approximate=True)
def _silu(x):
    return jax.nn.silu(x)
def _sigmoid(x):
    return jax.nn.sigmoid(x)
def _layernorm(x, axis=-1, eps=1e-5):
    m = jnp.mean(x, axis=axis, keepdims=True)
    v = jnp.var(x, axis=axis, keepdims=True)
    return (x - m) / jnp.sqrt(v + eps)
def _scatter_add(tgt, idx, src, axis=0):
    return tgt.at[idx].add(src)
def _segment_sum(src, seg, n):
    return jax.ops.segment_sum(src, seg, n)

kernel_name = 'mk_adj_resnorm_d1_adj_256_ed1123'

def setup_inputs(seed: int = 0):
    np.random.seed(seed)
    _w = jnp.asarray
    def _rec_inputs():
        import jax
        import jax.numpy as jnp
        _gk = jax.random.key(seed)
        x = -0.000929 + 1 * jax.random.normal(jax.random.fold_in(_gk, 1), (8192, 256), jnp.float32)
        _w = (1.0 + jnp.arange(8192, dtype=jnp.float32)) ** -0.5
        _w = _w / _w.mean()
        _pij = jnp.clip(0.000976562 * _w[:, None] * _w[None, :], 0.0, 1.0)
        _a = jax.random.uniform(jax.random.fold_in(_gk, 2), (8192, 8192)) < _pij
        adj = _a.astype(jnp.int32)
        return x, adj
    x, adj = _rec_inputs()
    def _L0_gnn_setup():
        import jax, jax.numpy as jnp
        import numpy as np
        N, IN_F, H, D = (4096, 256, 4, 64)
        NEG_SLOPE = 0.2
        key = jax.random.key(seed)
        ks = jax.random.split(key, 8)
        s_w = 1.0 / np.sqrt(H * D)
        s_u = 1.0
        return {'inputs': jax.random.normal(ks[0], (N, IN_F), jnp.float32), 'adj_mat': jax.random.randint(ks[1], (N, N), 0, 2, jnp.int32), 'weight': jax.random.normal(ks[2], (IN_F, H * D), jnp.float32) * s_w, 'weight_u': jax.random.normal(ks[3], (H, D, 1), jnp.float32) * s_u, 'weight_v': jax.random.normal(ks[4], (H, D, 1), jnp.float32) * s_u, 'bias': jax.random.normal(ks[5], (1, H * D), jnp.float32) * s_w, 'proj_w': jax.random.normal(ks[6], (H * D, IN_F), jnp.float32) * (1.0 / np.sqrt(IN_F)), 'proj_b': jax.random.normal(ks[7], (H * D,), jnp.float32) * (1.0 / np.sqrt(IN_F))}
    _L0_gnn_all = _L0_gnn_setup()
    _L0_gnn_in = {k: v for k, v in _L0_gnn_all.items() if k in ('weight', 'weight_u', 'weight_v', 'bias', 'proj_w', 'proj_b', )}
    del _L0_gnn_all

    return {
        "x": x,
        "adj": adj,
        "L0_gnn_weight": _L0_gnn_in["weight"],
        "L0_gnn_weight_u": _L0_gnn_in["weight_u"],
        "L0_gnn_weight_v": _L0_gnn_in["weight_v"],
        "L0_gnn_bias": _L0_gnn_in["bias"],
        "L0_gnn_proj_w": _L0_gnn_in["proj_w"],
        "L0_gnn_proj_b": _L0_gnn_in["proj_b"],
    }

def reference(x, adj, L0_gnn_weight, L0_gnn_weight_u, L0_gnn_weight_v, L0_gnn_bias, L0_gnn_proj_w, L0_gnn_proj_b):
    import jax
    import jax.numpy as jnp
    def _L0_gnn_ref(inputs, adj_mat, weight, weight_u, weight_v, bias, proj_w, proj_b):
        import jax, jax.numpy as jnp
        import numpy as np
        N, IN_F, H, D = (4096, 256, 4, 64)
        NEG_SLOPE = 0.2
        support = (inputs @ weight).reshape(-1, H, D).transpose(1, 0, 2)
        f1 = jnp.einsum('hnd,hd->hn', support, weight_u[..., 0])[:, None, :]
        f2 = jnp.einsum('hnd,hd->hn', support, weight_v[..., 0])[:, :, None]
        scores = jax.nn.leaky_relu(f1 + f2, NEG_SLOPE)
        masked = scores * adj_mat.astype(scores.dtype)
        mask = masked != 0
        neg_inf = jnp.asarray(-jnp.inf, masked.dtype)
        m = jnp.max(jnp.where(mask, masked, neg_inf), axis=2, keepdims=True)
        m = jnp.where(jnp.isfinite(m), m, jnp.zeros_like(m))
        e = jnp.where(mask, jnp.exp(masked - m), jnp.zeros_like(masked))
        denom = e.sum(axis=2, keepdims=True)
        attn = jnp.where(denom > 0, e / jnp.where(denom > 0, denom, 1.0), jnp.zeros_like(e))
        out = jnp.einsum('hnm,hmd->hnd', attn, support)
        out = out.transpose(1, 0, 2).reshape(-1, H * D)
        out = out + bias
        out = out + inputs @ proj_w.T + proj_b
        return out

    x = _layernorm(x + _L0_gnn_ref(x, adj, L0_gnn_weight, L0_gnn_weight_u, L0_gnn_weight_v, L0_gnn_bias, L0_gnn_proj_w, L0_gnn_proj_b), axis=-1)
    return x


_drawn_inputs = setup_inputs


def setup_inputs(seed=0):
    import zlib

    import numpy as np

    out = dict(_drawn_inputs(seed))
    spreads = {}
    factors = {}
    for name, (base, spread) in spreads.items():
        noise = np.random.default_rng([zlib.crc32(name.encode()), seed]).standard_normal(out[name].shape)
        drawn = base * np.exp(spread * noise) if base else spread * noise
        out[name] = jnp.asarray(drawn.astype(out[name].dtype))
    for name, factor in factors.items():
        out[name] = (out[name] * factor).astype(out[name].dtype)
    return out
```

```python
import concourse.bass as bass
from concourse import mybir
from concourse.alu_op_type import AluOpType as ALU
from contextlib import ExitStack


def build(nc, x, adj, weight, weight_u, weight_v, bias, proj_w, proj_b, out):
    fp32, bf16, i32 = mybir.dt.float32, mybir.dt.bfloat16, mybir.dt.int32
    ACT = mybir.ActivationFunctionType
    AX = mybir.AxisListType
    RMAX = bass.bass_isa.ReduceOp.max

    P = 128
    N, F = x.shape
    H, D = weight_u.shape[0], weight_u.shape[1]
    KT = F // P
    MT = N // P
    NC = 512
    J = NC // P
    CH = N // NC
    WH = D + 2
    UM = 512
    I = UM // P
    PAIRS = N // UM // 2
    PS = 2 * I
    SC = MT
    EB = 8
    TB = 4
    K = 30.0
    EPS = 1e-5
    NEG = 0.2

    adj_v = adj.rearrange("(c j p) (g m) -> c g p j m", j=J, p=P, m=UM)
    x_v = x.rearrange("(g j p) f -> g p j f", j=J, p=P)
    out_v = out.rearrange("(c j p) f -> c p j f", j=J, p=P)

    ctx = ExitStack()
    with ctx:
        def sb(name, shape, dt):
            return ctx.enter_context(nc.sbuf_tensor(name, shape, dt))

        def sem(name):
            return ctx.enter_context(nc.semaphore(name))

        r_dram = nc.dram_tensor("r_rows", [H, N], fp32, kind="Internal").ap()

        W = sb("W", [P, MT, H, WH], fp32)
        Y = sb("Y", [P, MT, F], fp32)
        q = sb("q", [P, MT, H], fp32)
        f2zero = sb("f2zero", [P, H, MT], fp32)
        adj_raw = sb("adj_raw", [P, 2, J, UM], i32)
        adj_bf = sb("adj_bf", [P, 2, J, UM], bf16)
        adjT = sb("adjT", [P, TB, NC], bf16)
        e = sb("e", [P, EB, NC], fp32)
        r = sb("r", [P, 2, H, NC], fp32)
        z = sb("z", [P, J, F], fp32)
        acc_sb = sb("acc_sb", [P, J, H, WH], fp32)
        ident = sb("ident", [P, P], fp32)
        ident_bf = sb("ident_bf", [P, P], bf16)
        zeros = sb("zeros", [P, H * WH], bf16)
        Bs = sb("Bs", [P, KT, F + 2 * H], fp32)
        PT = sb("PT", [P, KT, F], fp32)
        b_row = sb("b_row", [P, F], fp32)
        eps_t = sb("eps_t", [P, 1], fp32)
        mx = sb("mx", [P, H], fp32)
        cmax = sb("cmax", [P, H], fp32)
        nb_q = sb("nb_q", [P, H], fp32)
        nb_c = sb("nb_c", [P, H], fp32)
        rsum = sb("rsum", [P, J], fp32)
        nmean = sb("nmean", [P, J], fp32)
        ssq = sb("ssq", [P, J], fp32)
        std = sb("std", [P, J], fp32)
        rstd = sb("rstd", [P, J], fp32)
        nmr = sb("nmr", [P, J], fp32)
        den = sb("den", [P, J, H], fp32)
        dif = sb("dif", [P, J, H], fp32)
        pos = sb("pos", [P, J, H], fp32)
        rden = sb("rden", [P, J, H], fp32)
        x_in = e[:, 0:4, :].rearrange("p (b j) c -> p b (j c)", b=2).rearrange("p b (j f) -> p b j f", f=F)
        xT = e[:, 4:8, :].rearrange("p (b k) n -> p b k n", b=2)
        r0 = r[:, 0, :, :].rearrange("p h n -> p (h n)")
        r1 = r[:, 1, :, :].rearrange("p h n -> p (h n)")
        f_all = r0[:, 0:2 * H * MT].rearrange("p (h t) -> p h t", t=MT)
        C = r0[:, 512:512 + H * MT].rearrange("p (h t) -> p h t", t=MT)
        r_nat = r0[:, 1024:1024 + H * MT].rearrange("p (h t) -> p h t", t=MT)
        r_T = r0[:, 1536:1536 + H * MT].rearrange("p (k n) -> p k n", n=P)
        uv = r1[:, 0:2 * F].rearrange("p (w f) -> p w f", w=2)
        wuv = r1[:, 512:512 + F]
        b2 = acc_sb[:, 0, :, :].rearrange("p h w -> p (h w)")[:, 0:F]
        pw = acc_sb[:, 1:3, :, :].rearrange("p j h w -> p (j h w)")[:, 0:KT * F].rearrange(
            "p (k f) -> p k f", k=KT)
        psum = ctx.enter_context(nc.psum_tensor("psum", [P, 8, 512], fp32))
        acc = psum[:, 0:J, 0:H * WH]
        psT = [psum[:, 4 + b, 0:NC // 2].bitcast(bf16) for b in range(2)]
        ln_junk = psum[:, 6:8, :].rearrange("p b (j f) -> p (b j) f", f=F)

        x_loaded = [sem(f"x_loaded{b}") for b in range(2)]
        w_loaded = sem("w_loaded")
        consts = sem("consts")
        ident_z = sem("ident_z")
        ident_ok = sem("ident_ok")
        dve_step = sem("dve_step")
        B_ready = sem("B_ready")
        pwT_ready = sem("pwT_ready")
        PT_ready = sem("PT_ready")
        xT_psum = sem("xT_psum")
        xT_sb = sem("xT_sb")
        S_psum = sem("S_psum")
        Y_psum = sem("Y_psum")
        S_out = sem("S_out")
        Y_out = sem("Y_out")
        f1_max = sem("f1_max")
        c_ready = sem("c_ready")
        nb_ready = sem("nb_ready")
        C_ready = sem("C_ready")
        q_ready = sem("q_ready")
        r_ready = sem("r_ready")
        rT_psum = sem("rT_psum")
        rT_sb = sem("rT_sb")
        r_stored = sem("r_stored")
        W_ready = sem("W_ready")
        r_loaded = [sem(f"r_loaded{b}") for b in range(2)]
        adj_loaded = [sem(f"adj_loaded{b}") for b in range(2)]
        adj_cast = sem("adj_cast")
        adjT_psum = sem("adjT_psum")
        adjT_ready = sem("adjT_ready")
        e_ready = sem("e_ready")
        e_used = sem("e_used")
        acc_done = sem("acc_done")
        acc_copied = sem("acc_copied")
        z_ready = sem("z_ready")
        act_step = sem("act_step")
        std_ready = sem("std_ready")
        rstd_half = sem("rstd_half")
        rstd_ready = sem("rstd_ready")
        rden_ready = sem("rden_ready")
        out_ready = sem("out_ready")
        out_stored = sem("out_stored")

        block = ctx.enter_context(nc.Block())

        @block.sync
        def _(sp):
            sp.dma_start(Bs[:, :, 0:F], weight.rearrange("(k p) c -> p k c", p=P)).then_inc(w_loaded, 16)
            sp.dma_start(pw, proj_w.rearrange("(k p) c -> p k c", p=P)).then_inc(w_loaded, 16)
            sp.dma_start(uv[:, 0, :], weight_u.rearrange("h d o -> (o h d)").partition_broadcast(P)).then_inc(w_loaded, 16)
            sp.dma_start(uv[:, 1, :], weight_v.rearrange("h d o -> (o h d)").partition_broadcast(P)).then_inc(w_loaded, 16)
            sp.dma_start(b_row[:, :], bias[0, :].partition_broadcast(P)).then_inc(w_loaded, 16)
            sp.dma_start(b2, proj_b.partition_broadcast(P)).then_inc(w_loaded, 16)
            for g in range(2):
                sp.dma_start(x_in[:, g, :, :], x_v[g]).then_inc(x_loaded[g], 16)

            def load_unit(c, g, b):
                sp.dma_start(adj_raw[:, b, :, :], adj_v[c, g]).then_inc(adj_loaded[b], 16)

            load_unit(0, 0, 0)
            load_unit(0, 1, 1)
            with sp.Fori(1, CH // 2) as gg:
                for b in range(2):
                    sp.wait_ge(xT_psum, gg * 2 + (b - 1))
                    sp.dma_start(x_in[:, b, :, :], x_v[gg * 2 + b]).then_inc(x_loaded[b], 16)
            sp.wait_ge(rT_sb, 1)
            sp.dma_start(r_dram.rearrange("h (t p) -> (h t) p", p=P).rearrange("(k q) p -> q k p", q=P),
                         r_T).then_inc(r_stored, 16)
            sp.wait_ge(r_stored, 16)

            def load_r(c, b):
                src = r_dram.rearrange("h (c n) -> c h n", n=NC)[c].partition_broadcast(P)
                sp.dma_start(r[:, b, :, :], src).then_inc(r_loaded[b], 16)

            sp.wait_ge(W_ready, 1)
            load_r(0, 0)

            def load_pair(c, gp):
                u = (c * PAIRS + gp) * 2
                sp.wait_ge(adj_cast, u - 1)
                load_unit(c, gp * 2, 0)
                sp.wait_ge(adj_cast, u)
                load_unit(c, gp * 2 + 1, 1)

            def chunk_tail(c):
                with sp.Fori(1, PAIRS) as gp:
                    load_pair(c, gp)

            def next_r(c, b):
                sp.wait_ge(e_ready, c * (SC * H))
                load_r(c + 1, b)

            with sp.Fori(0, CH // 2 - 1) as cc:
                for h in range(2):
                    c = cc * 2 + h
                    next_r(c, 1 - h)
                    chunk_tail(c)
                    load_pair(c + 1, 0)
            next_r(CH - 2, 1)
            chunk_tail(CH - 2)
            load_pair(CH - 1, 0)
            chunk_tail(CH - 1)

        @block.gpsimd
        def _(pool):
            nc.gpsimd.memset(ident[:, :], 0.0).then_inc(ident_z, 1)
            pool.wait_ge(ident_z, 1)
            nc.gpsimd.affine_select(out=ident[:, :], in_=ident[:, :], compare_op=ALU.not_equal, fill=1.0,
                                    base=0, pattern=[[-1, P]], channel_multiplier=1).then_inc(ident_ok, 1)
            pool.wait_ge(f1_max, 1)
            nc.gpsimd.partition_all_reduce(cmax[:, :], mx[:, :], P, RMAX).then_inc(c_ready, 1)
            with pool.Fori(0, CH) as c:
                pool.wait_ge(out_ready, c + 1)
                pool.dma_start(out_v[c], z[:, :, :]).then_inc(out_stored, 16)
            pool.wait_ge(out_stored, 16 * CH)

        @block.scalar
        def _(act):
            def cast_unit(u, pair, b):
                act.wait_ge(adj_loaded[b], pair * 16 + 16)
                act.wait_ge(adjT_psum, (u - 1) * I)
                nc.scalar.copy(adj_bf[:, b, :, :], adj_raw[:, b, :, :]).then_inc(adj_cast, 1)

            with act.Fori(0, CH) as g:
                for j in range(J):
                    act.wait_ge(S_psum, g * J + (j + 1))
                    nc.scalar.copy(W[:, bass.ds(g * J + j, 1), :, 0:D].rearrange("p t h d -> p (t h) d"),
                                   psum[:, j % 2, 0:F].rearrange("p (h d) -> p h d", d=D)).then_inc(S_out, 1)
                    nc.scalar.copy(f_all[:, :, bass.ds(g * J + j, 1)].rearrange("p h t -> p (h t)"),
                                   psum[:, j % 2, F:F + 2 * H]).then_inc(S_out, 1)
            act.wait_ge(adj_loaded[0], 16)
            nc.scalar.copy(adj_bf[:, 0, :, :], adj_raw[:, 0, :, :]).then_inc(adj_cast, 1)
            act.wait_ge(nb_ready, 1)
            for h in range(H):
                nc.scalar.activation(r_nat[:, h, :], f_all[:, H + h, :], ACT.Exp, bias=nb_q[:, h:h + 1],
                                     scale=-(1 - NEG)).then_inc(r_ready, 1)
            for h in range(H):
                nc.scalar.activation(C[:, h, :], f_all[:, h, :], ACT.Exp, bias=nb_c[:, h:h + 1],
                                     scale=NEG).then_inc(C_ready, 1)
            for h in range(H):
                nc.scalar.activation(q[:, :, h], f_all[:, h, :], ACT.Exp, bias=nb_q[:, h:h + 1],
                                     scale=1 - NEG).then_inc(q_ready, 1)
            act.wait_ge(rT_psum, 1)
            nc.scalar.copy(r_T, psum[:, 6, 0:H * MT].rearrange("p (k n) -> p k n", n=P)).then_inc(rT_sb, 1)

            def evac(s, k, first):
                act.wait_ge(adjT_psum, s + 1)
                if not (first and k < TB):
                    act.wait_ge(e_ready, (s - (TB - 1)) * H)
                nc.scalar.copy(adjT[:, k % TB, :], psT[k % 2]).then_inc(adjT_ready, 1)

            def acc_copy(c):
                act.wait_ge(acc_done, c + 1)
                act.wait_ge(z_ready, c)
                nc.scalar.copy(acc_sb[:, :, :, :].rearrange("p j h w -> p j (h w)"), acc).then_inc(acc_copied, 1)

            def layer_norm(c):
                def done(ins, k):
                    ins.then_inc(act_step, 1)
                    act.wait_ge(act_step, c * 3 + k)

                act.wait_ge(z_ready, c + 1)
                for j in range(J):
                    last = nc.scalar.activation(ln_junk[:, j, :], z[:, j, :],
                                                ACT.Identity, accum_out=rsum[:, j:j + 1])
                done(last, 1)
                done(nc.scalar.mul(nmean[:, :], rsum[:, :], -1.0 / F), 2)
                for j in range(J):
                    last = nc.scalar.activation(ln_junk[:, j, :], z[:, j, :],
                                                ACT.Square, bias=nmean[:, j:j + 1], accum_out=ssq[:, j:j + 1])
                done(last, 3)
                nc.scalar.activation(std[:, :], ssq[:, :], ACT.Sqrt, bias=eps_t[:, 0:1], scale=1.0 / F).then_inc(std_ready, 1)
                act.wait_ge(rstd_ready, c + 1)
                for j in range(J):
                    last = nc.scalar.activation(z[:, j, :], z[:, j, :], ACT.Identity, bias=nmr[:, j:j + 1], scale=rstd[:, j:j + 1])
                last.then_inc(out_ready, 1)

            def pair(c, gp, first=False, last=False, head=False):
                p = c * PAIRS + gp
                if first:
                    act.wait_ge(adj_loaded[1], 16)
                    nc.scalar.copy(adj_bf[:, 1, :, :], adj_raw[:, 1, :, :]).then_inc(adj_cast, 1)
                else:
                    cast_unit(p * 2 + 1, p, 1)
                for k in range(PS):
                    evac(p * PS + k, k, first)
                    if k == I - 1 and not last:
                        cast_unit(p * 2 + 2, p + 1, 0)
                    if k == 2 and head:
                        acc_copy(c - 1)
                if head:
                    layer_norm(c - 1)

            def chunk_tail(c):
                with act.Fori(1, PAIRS) as gp:
                    pair(c, gp)

            pair(0, 0, first=True)
            with act.Fori(0, CH - 1) as c:
                chunk_tail(c)
                pair(c + 1, 0, head=True)
            with act.Fori(1, PAIRS - 1) as gp:
                pair(CH - 1, gp)
            pair(CH - 1, PAIRS - 1, last=True)
            acc_copy(CH - 1)
            layer_norm(CH - 1)

        @block.vector
        def _(dve):
            links = [0]

            def link(ins):
                links[0] += 1
                ins.then_inc(dve_step, 1)
                dve.wait_ge(dve_step, links[0])

            nc.vector.memset(zeros[:, :], 0.0).then_inc(consts, 1)
            nc.vector.memset(eps_t[:, :], EPS).then_inc(consts, 1)
            dve.wait_ge(ident_ok, 1)
            nc.vector.tensor_copy(ident_bf[:, :], ident[:, :]).then_inc(consts, 1)
            dve.wait_ge(w_loaded, 96)
            link(nc.vector.tensor_tensor(b_row[:, :], b_row[:, :], b2, ALU.add))
            for k in range(KT):
                for w in range(2):
                    link(nc.vector.tensor_tensor(wuv, Bs[:, k, 0:F], uv[:, w, :], ALU.mult))
                    ins = nc.vector.tensor_reduce(Bs[:, k, F + w * H:F + (w + 1) * H],
                                                  wuv.rearrange("p (h d) -> p h d", d=D), AX.X, ALU.add)
                    if k == KT - 1 and w == 1:
                        ins.then_inc(B_ready, 1)
                    else:
                        link(ins)
            dve.wait_ge(pwT_ready, 1)
            link(nc.vector.tensor_copy(PT[:, :, :], psum[:, 6, :].rearrange("p (k f) -> p k f", k=KT)))
            for k in range(KT):
                blk = PT[:, k, k * P:(k + 1) * P]
                nc.vector.tensor_tensor(blk, blk, ident[:, :], ALU.add).then_inc(PT_ready, 1)
            with dve.Fori(0, CH // 2) as gg:
                for b in range(2):
                    g = gg * 2 + b
                    dve.wait_ge(xT_psum, g + 1)
                    nc.vector.tensor_copy(xT[:, b, :, :], psum[:, 4:4 + KT, :]).then_inc(xT_sb, 1)
                    for j in range(J):
                        t = g * J + j
                        dve.wait_ge(Y_psum, t + 1)
                        nc.vector.tensor_tensor(Y[:, bass.ds(t, 1), :].rearrange("p t f -> p (t f)"),
                                                psum[:, 2 + j % 2, 0:F], b_row[:, :], ALU.add).then_inc(Y_out, 1)
            dve.wait_ge(S_out, 2 * MT)
            nc.vector.tensor_reduce(mx[:, :], f_all[:, 0:H, :], AX.X, ALU.max).then_inc(f1_max, 1)
            dve.wait_ge(c_ready, 1)
            link(nc.vector.tensor_scalar(nb_q[:, :], cmax[:, :], -(1 - NEG), K, ALU.mult, ALU.add))
            nc.vector.tensor_scalar(nb_c[:, :], cmax[:, :], -NEG, None, ALU.mult).then_inc(nb_ready, 1)
            nc.vector.tensor_scalar(f2zero[:, :, :], f_all[:, H:2 * H, :], 0.0, None, ALU.is_equal)
            for h in range(H):
                dve.wait_ge(C_ready, h + 1)
                Wh = W[:, :, h, 0:D]
                nc.vector.tensor_tensor(Wh, Wh, C[:, h, :].unsqueeze(2).to_broadcast([P, MT, D]), ALU.mult)
                nc.vector.tensor_copy(W[:, :, h, D], C[:, h, :])
                ins = nc.vector.scalar_tensor_tensor(W[:, :, h, D + 1], f_all[:, h, :], 0.0, C[:, h, :],
                                                     ALU.not_equal, ALU.mult)
            ins.then_inc(W_ready, 1)
            dve.wait_ge(q_ready, H)

            def step(s, k, mt, b, first):
                dve.wait_ge(adjT_ready, s + 1)
                for h in range(H):
                    if not (first and k < EB // H):
                        dve.wait_ge(e_used, s * H + (h - EB + 1))
                    nc.vector.scalar_tensor_tensor(
                        e[:, (k * H + h) % EB, :], r[:, b, h, :],
                        q[:, bass.ds(mt, 1), h],
                        adjT[:, k % TB, :], ALU.max, ALU.mult).then_inc(e_ready, 1)

            def epilogue(c):
                dve.wait_ge(acc_copied, c + 1)
                n = [0]

                def small(ins):
                    n[0] += 1
                    ins.then_inc(dve_step, 1)
                    dve.wait_ge(dve_step, links[0] + c * 5 + n[0])

                d1, d2 = acc_sb[:, :, :, D], acc_sb[:, :, :, D + 1]
                z0 = f2zero[:, :, bass.ds(c * J, J)].rearrange("p h j -> p j h")
                small(nc.vector.tensor_tensor(dif[:, :, :], d2, d1, ALU.subtract))
                small(nc.vector.tensor_tensor(dif[:, :, :], dif[:, :, :], z0, ALU.mult))
                small(nc.vector.tensor_tensor(den[:, :, :], d1, dif[:, :, :], ALU.add))
                small(nc.vector.tensor_scalar(pos[:, :, :], den[:, :, :], 1e-37, None, ALU.max))
                nc.vector.tensor_scalar(dif[:, :, :], den[:, :, :], 0.0, None, ALU.is_gt)
                small(nc.vector.reciprocal(rden[:, :, :], pos[:, :, :]))
                nc.vector.tensor_tensor(rden[:, :, :], rden[:, :, :], dif[:, :, :], ALU.mult).then_inc(rden_ready, 1)
                dve.wait_ge(rden_ready, c + 1)
                dve.wait_ge(out_stored, c * 16)
                for j in range(J):
                    for h in range(H):
                        y = Y[:, bass.ds(c * J + j, 1), h * D:(h + 1) * D].rearrange("p t f -> p (t f)")
                        ins = nc.vector.scalar_tensor_tensor(z[:, j, h * D:(h + 1) * D], acc_sb[:, j, h, 0:D], rden[:, j, h:h + 1], y,
                                                             ALU.mult, ALU.add)
                ins.then_inc(z_ready, 1)

            def rstd_part(c):
                dve.wait_ge(std_ready, c + 1)
                nc.vector.reciprocal(rstd[:, :], std[:, :]).then_inc(rstd_half, 1)
                dve.wait_ge(rstd_half, c + 1)
                nc.vector.tensor_tensor(nmr[:, :], nmean[:, :], rstd[:, :], ALU.mult).then_inc(rstd_ready, 1)

            def pair(c, gp, b, first=False, head=False):
                p = c * PAIRS + gp
                for k in range(PS):
                    step(p * PS + k, k, gp * PS + k, b, first)
                    if head and k == 3:
                        epilogue(c - 1)
                    if head and k == 5:
                        rstd_part(c - 1)

            def chunk_tail(c, b):
                with dve.Fori(1, PAIRS) as gp:
                    pair(c, gp, b)

            dve.wait_ge(r_loaded[0], 16)
            pair(0, 0, 0, first=True)
            with dve.Fori(0, CH // 2 - 1) as cc:
                for h in range(2):
                    c = cc * 2 + h
                    chunk_tail(c, h)
                    dve.wait_ge(r_loaded[1 - h], cc * 16 + 16 * (1 + h))
                    pair(c + 1, 0, 1 - h, head=True)
            chunk_tail(CH - 2, 0)
            dve.wait_ge(r_loaded[1], 16 * (CH // 2))
            pair(CH - 1, 0, 1, head=True)
            chunk_tail(CH - 1, 1)
            epilogue(CH - 1)
            rstd_part(CH - 1)

        @block.tensor
        def _(pe):
            pe.wait_ge(ident_ok, 1)
            pe.wait_ge(w_loaded, 96)
            for ki in range(KT):
                for ko in range(KT):
                    last = nc.tensor.transpose(psum[:, 6, ki * F + ko * P:ki * F + (ko + 1) * P],
                                               pw[:, ko, ki * P:(ki + 1) * P], ident[:, :])
            last.then_inc(pwT_ready, 1)
            pe.wait_ge(B_ready, 1)
            pe.wait_ge(PT_ready, KT)

            def x_transposes(g, b):
                for j in range(J):
                    for k in range(KT):
                        last = nc.tensor.transpose(psum[:, 4 + k, j * P:(j + 1) * P],
                                                   x_in[:, b, j, k * P:(k + 1) * P], ident[:, :])
                last.then_inc(xT_psum, 1)

            def products(g, b, first):
                pe.wait_ge(xT_sb, g + 1)
                for j in range(J):
                    t = g * J + j
                    if not (first and j < 2):
                        pe.wait_ge(S_out, (t - 1) * 2)
                    for k in range(KT):
                        last = nc.tensor.matmul(psum[:, j % 2, 0:F + 2 * H], xT[:, b, k, j * P:(j + 1) * P],
                                                Bs[:, k, :], start=(k == 0), stop=(k == KT - 1))
                    last.then_inc(S_psum, 1)
                    if not (first and j < 2):
                        pe.wait_ge(Y_out, t - 1)
                    for k in range(KT):
                        last = nc.tensor.matmul(psum[:, 2 + j % 2, 0:F], xT[:, b, k, j * P:(j + 1) * P],
                                                PT[:, k, :], start=(k == 0), stop=(k == KT - 1))
                    last.then_inc(Y_psum, 1)

            pe.wait_ge(x_loaded[0], 16)
            x_transposes(0, 0)
            products(0, 0, True)
            pe.wait_ge(x_loaded[1], 16)
            x_transposes(1, 1)
            products(1, 1, False)
            with pe.Fori(1, CH // 2) as gg:
                for b in range(2):
                    pe.wait_ge(x_loaded[b], gg * 16 + 16)
                    x_transposes(gg * 2 + b, b)
                    products(gg * 2 + b, b, False)
            pe.wait_ge(r_ready, H)
            for k in range(H * MT // P):
                last = nc.tensor.transpose(psum[:, 6, k * P:(k + 1) * P],
                                           r_nat.rearrange("p h t -> p (h t)")[:, k * P:(k + 1) * P], ident[:, :])
            last.then_inc(rT_psum, 1)

            def transposes(s, k, u):
                if k % I == 0:
                    pe.wait_ge(adj_cast, u + 1)
                b, i = (k // I) % 2, k % I
                for j in range(J):
                    last = nc.tensor.transpose(psT[k % 2][:, j * P:(j + 1) * P],
                                               adj_bf[:, b, j, i * P:(i + 1) * P], ident_bf[:, :])
                last.then_inc(adjT_psum, 1)

            def pair(c, gp, head=False, first=False, last_pair=False):
                p = c * PAIRS + gp
                for k in range(PS):
                    s = p * PS + k
                    if not (last_pair and k + 2 >= PS):
                        pe.wait_ge(adjT_ready, s + 1)
                        transposes(s + 2, k + 2, p * 2 + (k + 2) // I)
                    if k == 0 and (head or first):
                        if head:
                            pe.wait_ge(acc_copied, c)
                        for j in range(J):
                            nc.tensor.matmul(psum[:, j, 0:H * WH], zeros[:, 0:P], zeros[:, :], start=True, stop=False,
                                             skip_group_check=True)
                    for h in range(H):
                        pe.wait_ge(e_ready, s * H + (h + 1))
                        slot = (k * H + h) % EB
                        for j in range(J):
                            last = nc.tensor.matmul(psum[:, j, h * WH:(h + 1) * WH], e[:, slot, j * P:(j + 1) * P],
                                                    W[:, bass.ds(gp * PS + k, 1), h, :].rearrange("p t w -> p (t w)"),
                                                    start=False, stop=False, skip_group_check=True)
                        last.then_inc(e_used, 1)

            def chunk_end():
                for j in range(J):
                    last = nc.tensor.matmul(psum[:, j, 0:H * WH], zeros[:, 0:P], zeros[:, :], start=False, stop=True,
                                            skip_group_check=True)
                last.then_inc(acc_done, 1)

            pe.wait_ge(consts, 3)
            transposes(0, 0, 0)
            transposes(1, 1, 0)
            pe.wait_ge(S_out, 2 * MT)
            pe.wait_ge(Y_out, MT)
            pe.wait_ge(W_ready, 1)
            pair(0, 0, first=True)
            with pe.Fori(0, CH - 1) as c:
                with pe.Fori(1, PAIRS) as gp:
                    pair(c, gp)
                chunk_end()
                pair(c + 1, 0, head=True)
            with pe.Fori(1, PAIRS - 1) as gp:
                pair(CH - 1, gp)
            pair(CH - 1, PAIRS - 1, last_pair=True)
            chunk_end()


_INS = ["x", "adj", "L0_gnn_weight", "L0_gnn_weight_u", "L0_gnn_weight_v", "L0_gnn_bias", "L0_gnn_proj_w",
        "L0_gnn_proj_b"]


def kernel(**inputs):
    import numpy as _np
    import concourse.bacc as _bacc
    from concourse import mybir as _mybir
    from concourse.bass_utils import run_bass_kernel_spmd as _run

    nc = _bacc.Bacc("TRN2", target_bir_lowering=False, num_devices=1)
    arrays, args = {}, []
    for name in _INS:
        a = _np.ascontiguousarray(inputs[name])
        arrays[f"in_{name}"] = a
        args.append(nc.dram_tensor(f"in_{name}", a.shape, _mybir.dt.from_np(a.dtype), kind="ExternalInput").ap())
    out = nc.dram_tensor("out", inputs["x"].shape, _mybir.dt.float32, kind="ExternalOutput").ap()
    build(nc, *args, out)
    r = _run(nc, [arrays], core_ids=[0])
    return r.results[0]["out"]
```

```python
import concourse.bass as bass
from concourse import mybir
from concourse.alu_op_type import AluOpType as ALU
from contextlib import ExitStack


def build(nc, x, adj, weight, weight_u, weight_v, bias, proj_w, proj_b, out):
    fp32, bf16, i32 = mybir.dt.float32, mybir.dt.bfloat16, mybir.dt.int32
    ACT = mybir.ActivationFunctionType
    AX = mybir.AxisListType
    RMAX = bass.bass_isa.ReduceOp.max

    P = 128
    N, F = x.shape
    H, D = weight_u.shape[0], weight_u.shape[1]
    KT = F // P
    MT = N // P
    NC = 512
    J = NC // P
    CH = N // NC
    WH = D + 2
    DT = 32
    WR = 4
    NB = 3
    UM = 512
    I = UM // P
    PAIRS = N // UM // 2
    PS = 2 * I
    SC = MT
    EB = 8
    K = 30.0
    EPS = 1e-5
    NEG = 0.2

    adj_v = adj.rearrange("(c j p) (g m) -> c g p j m", j=J, p=P, m=UM)
    x_v = x.rearrange("(g j p) f -> g p j f", j=J, p=P)
    out_v = out.rearrange("(c j p) f -> c p j f", j=J, p=P)

    ctx = ExitStack()
    with ctx:
        def sb(name, shape, dt):
            return ctx.enter_context(nc.sbuf_tensor(name, shape, dt))

        def sem(name):
            return ctx.enter_context(nc.semaphore(name))

        r_dram = nc.dram_tensor("r_rows", [H, N], fp32, kind="Internal").ap()

        W = sb("W", [P, MT, H, WH], fp32)
        Y = sb("Y", [P, MT, F], fp32)
        q = sb("q", [P, MT, H], fp32)
        f2zero = sb("f2zero", [P, H, MT], fp32)
        adj_raw = sb("adj_raw", [P, 2, J, UM], i32)
        adj_bf = sb("adj_bf", [P, J * UM], bf16)
        adjT = sb("adjT", [P, 2, J, I, P], bf16)
        e = sb("e", [P, EB, NC], fp32)
        r = sb("r", [P, 2, H, NC], fp32)
        sumT = sb("sumT", [P, NB, NC], fp32)
        z = sumT[:, 0:2, :].rearrange("p b (j f) -> p (b j) f", f=F)
        Wt = sb("Wt", [P, WR, H, D + DT], fp32)
        ident = sb("ident", [P, P], fp32)
        zeros = sb("zeros", [P, NC], bf16)
        eps_t = sb("eps_t", [P, 1], fp32)
        mx = sb("mx", [P, H], fp32)
        cmax = sb("cmax", [P, H], fp32)
        nb_q = sb("nb_q", [P, H], fp32)
        nb_c = sb("nb_c", [P, H], fp32)
        rsum = sb("rsum", [P, J], fp32)
        nmean = sb("nmean", [P, J], fp32)
        ssq = sb("ssq", [P, J], fp32)
        std = sb("std", [P, J], fp32)
        rstd = sb("rstd", [P, J], fp32)
        nmr = sb("nmr", [P, J], fp32)
        den = sb("den", [P, J, H], fp32)
        dif = sb("dif", [P, J, H], fp32)
        pos = sb("pos", [P, J, H], fp32)
        rden = sb("rden", [P, J, H], fp32)
        x_in = e[:, 0:4, :].rearrange("p (b j) c -> p b (j c)", b=2).rearrange("p b (j f) -> p b j f", f=F)
        xT = e[:, 4:8, :].rearrange("p (b k) n -> p b k n", b=2)
        r0 = r[:, 0, :, :].rearrange("p h n -> p (h n)")
        r1 = r[:, 1, :, :].rearrange("p h n -> p (h n)")
        f_all = r0[:, 0:2 * H * MT].rearrange("p (h t) -> p h t", t=MT)
        C = r0[:, 512:512 + H * MT].rearrange("p (h t) -> p h t", t=MT)
        r_nat = r0[:, 1024:1024 + H * MT].rearrange("p (h t) -> p h t", t=MT)
        r_T = r0[:, 1536:1536 + H * MT].rearrange("p (k n) -> p k n", n=P)
        uv = r1[:, 0:2 * F].rearrange("p (w f) -> p w f", w=2)
        wuv = r1[:, 512:512 + F]
        b2 = sumT[:, 0, 0:F]
        b_row = sumT[:, 0, F:2 * F]
        pw = sumT[:, 1, :].rearrange("p (k f) -> p k f", k=KT)
        Wt_flat = Wt[:, :, :, :].rearrange("p r h w -> p (r h w)")
        BW = F + 2 * H
        Bs = Wt_flat[:, 0:KT * BW].rearrange("p (k c) -> p k c", k=KT)
        PT = Wt_flat[:, KT * BW:KT * (BW + F)].rearrange("p (k c) -> p k c", k=KT)
        psum = ctx.enter_context(nc.psum_tensor("psum", [P, 8, 512], fp32))
        def bank(par, i):
            return psum[:, par * NB + i, :]


        x_loaded = [sem(f"x_loaded{b}") for b in range(2)]
        w_loaded = sem("w_loaded")
        consts = sem("consts")
        ident_z = sem("ident_z")
        ident_ok = sem("ident_ok")
        dve_step = sem("dve_step")
        B_ready = sem("B_ready")
        pwT_ready = sem("pwT_ready")
        PT_ready = sem("PT_ready")
        xT_psum = sem("xT_psum")
        xT_sb = sem("xT_sb")
        S_psum = sem("S_psum")
        Y_psum = sem("Y_psum")
        S_out = sem("S_out")
        Y_out = sem("Y_out")
        f1_max = sem("f1_max")
        c_ready = sem("c_ready")
        nb_ready = sem("nb_ready")
        C_ready = sem("C_ready")
        q_ready = sem("q_ready")
        r_ready = sem("r_ready")
        rT_psum = sem("rT_psum")
        rT_sb = sem("rT_sb")
        r_stored = sem("r_stored")
        W_ready = sem("W_ready")
        r_loaded = [sem(f"r_loaded{b}") for b in range(2)]
        adj_loaded = [sem(f"adj_loaded{b}") for b in range(2)]
        adj_cast = sem("adj_cast")
        adjT_loaded = [sem(f"adjT_loaded{b}") for b in range(2)]
        e_ready = sem("e_ready")
        e_used = sem("e_used")
        Wt_ready = sem("Wt_ready")
        Wt_zero = sem("Wt_zero")
        sums_done = sem("sums_done")
        sumT_ready = sem("sumT_ready")
        sums_psum = sem("sums_psum")
        z_ready = sem("z_ready")
        act_step = sem("act_step")
        std_ready = sem("std_ready")
        rstd_ready = sem("rstd_ready")
        nmr_ready = sem("nmr_ready")
        rden_ready = sem("rden_ready")
        out_ready = sem("out_ready")
        out_stored = sem("out_stored")

        block = ctx.enter_context(nc.Block())

        @block.sync
        def _(sp):
            sp.dma_start(Bs[:, :, 0:F], weight.rearrange("(k p) c -> p k c", p=P)).then_inc(w_loaded, 16)
            sp.dma_start(pw, proj_w.rearrange("(k p) c -> p k c", p=P)).then_inc(w_loaded, 16)
            sp.dma_start(uv[:, 0, :], weight_u.rearrange("h d o -> (o h d)").partition_broadcast(P)).then_inc(w_loaded, 16)
            sp.dma_start(uv[:, 1, :], weight_v.rearrange("h d o -> (o h d)").partition_broadcast(P)).then_inc(w_loaded, 16)
            sp.dma_start(b_row[:, :], bias[0, :].partition_broadcast(P)).then_inc(w_loaded, 16)
            sp.dma_start(b2, proj_b.partition_broadcast(P)).then_inc(w_loaded, 16)
            for g in range(2):
                sp.dma_start(x_in[:, g, :, :], x_v[g]).then_inc(x_loaded[g], 16)

            def load_unit(c, g, b):
                sp.dma_start(adj_raw[:, b, :, :], adj_v[c, g]).then_inc(adj_loaded[b], 16)

            def transpose_unit(b):
                sp.dma_start(adjT[:, b, :, :, :].rearrange("p j i n -> p (j i) n"), adj_bf[:, :],
                             transpose=True).then_inc(adjT_loaded[b], 16)

            load_unit(0, 0, 0)
            load_unit(0, 1, 1)
            with sp.Fori(1, CH // 2) as gg:
                for b in range(2):
                    sp.wait_ge(xT_psum, gg * 2 + (b - 1))
                    sp.dma_start(x_in[:, b, :, :], x_v[gg * 2 + b]).then_inc(x_loaded[b], 16)
            sp.wait_ge(adj_cast, 1)
            transpose_unit(0)
            sp.wait_ge(rT_sb, 1)
            sp.dma_start(r_dram.rearrange("h (t p) -> (h t) p", p=P).rearrange("(k q) p -> q k p", q=P),
                         r_T).then_inc(r_stored, 16)
            sp.wait_ge(r_stored, 16)

            def load_r(c, b):
                src = r_dram.rearrange("h (c n) -> c h n", n=NC)[c].partition_broadcast(P)
                sp.dma_start(r[:, b, :, :], src).then_inc(r_loaded[b], 16)

            sp.wait_ge(W_ready, 1)
            load_r(0, 0)

            def first_units():
                for b in range(2):
                    sp.wait_ge(adj_cast, 2 + b)
                    if b:
                        sp.wait_ge(e_ready, I * H)
                    load_unit(0, 2 + b, b)
                    transpose_unit(1 - b)

            def load_pair(c, gp):
                u = (c * PAIRS + gp) * 2
                for b in range(2):
                    sp.wait_ge(adj_cast, u + b)
                    sp.wait_ge(e_ready, (u + (b - 2)) * (I * H))
                    load_unit(c, gp * 2 + b, b)
                    transpose_unit(1 - b)

            def chunk_tail(c):
                with sp.Fori(1, PAIRS) as gp:
                    load_pair(c, gp)

            def next_r(c, b, first=False):
                if not first:
                    sp.wait_ge(e_ready, c * (SC * H))
                load_r(c + 1, b)

            def two_chunks(cc):
                for par in range(2):
                    c = cc * 2 + par
                    chunk_tail(c)
                    next_r(c, 1 - par)
                    load_pair(c + 1, 0)

            first_units()
            with sp.Fori(2, PAIRS) as gp:
                load_pair(0, gp)
            next_r(0, 1, first=True)
            load_pair(1, 0)
            chunk_tail(1)
            next_r(1, 0)
            load_pair(2, 0)
            with sp.Fori(1, CH // 2 - 1) as cc:
                two_chunks(cc)
            chunk_tail(CH - 2)
            next_r(CH - 2, 1)
            load_pair(CH - 1, 0)
            chunk_tail(CH - 1)
            sp.wait_ge(adj_cast, CH * PAIRS * 2)
            sp.wait_ge(e_ready, (CH * PAIRS * 2 - 2) * (I * H))
            transpose_unit(1)

        @block.gpsimd
        def _(pool):
            nc.gpsimd.memset(ident[:, :], 0.0).then_inc(ident_z, 1)
            pool.wait_ge(ident_z, 1)
            nc.gpsimd.affine_select(out=ident[:, :], in_=ident[:, :], compare_op=ALU.not_equal, fill=1.0,
                                    base=0, pattern=[[-1, P]], channel_multiplier=1).then_inc(ident_ok, 1)
            pool.wait_ge(f1_max, 1)
            nc.gpsimd.partition_all_reduce(cmax[:, :], mx[:, :], P, RMAX).then_inc(c_ready, 1)
            with pool.Fori(0, CH) as c:
                pool.wait_ge(out_ready, c + 1)
                pool.dma_start(out_v[c], z[:, :, :]).then_inc(out_stored, 16)
            pool.wait_ge(out_stored, 16 * CH)

        @block.scalar
        def _(act):
            def cast_unit(pair, b, first=False):
                act.wait_ge(adj_loaded[b], pair * 16 + 16)
                if not (first and b == 0):
                    act.wait_ge(adjT_loaded[1 - b], (pair + b) * 16)
                nc.scalar.copy(adj_bf[:, :], adj_raw[:, b, :, :].rearrange("p j m -> p (j m)")).then_inc(adj_cast, 1)

            with act.Fori(0, CH) as g:
                for j in range(J):
                    act.wait_ge(S_psum, g * J + (j + 1))
                    nc.scalar.copy(W[:, bass.ds(g * J + j, 1), :, 0:D].rearrange("p t h d -> p (t h) d"),
                                   psum[:, j % 2, 0:F].rearrange("p (h d) -> p h d", d=D)).then_inc(S_out, 1)
                    nc.scalar.copy(f_all[:, :, bass.ds(g * J + j, 1)].rearrange("p h t -> p (h t)"),
                                   psum[:, j % 2, F:F + 2 * H]).then_inc(S_out, 1)
            cast_unit(0, 0, first=True)
            act.wait_ge(nb_ready, 1)
            for h in range(H):
                nc.scalar.activation(r_nat[:, h, :], f_all[:, H + h, :], ACT.Exp, bias=nb_q[:, h:h + 1],
                                     scale=-(1 - NEG)).then_inc(r_ready, 1)
            for h in range(H):
                nc.scalar.activation(C[:, h, :], f_all[:, h, :], ACT.Exp, bias=nb_c[:, h:h + 1],
                                     scale=NEG).then_inc(C_ready, 1)
            for h in range(H):
                nc.scalar.activation(q[:, :, h], f_all[:, h, :], ACT.Exp, bias=nb_q[:, h:h + 1],
                                     scale=1 - NEG).then_inc(q_ready, 1)
            act.wait_ge(rT_psum, 1)
            nc.scalar.copy(r_T, psum[:, 5, 0:H * MT].rearrange("p (k n) -> p k n", n=P)).then_inc(rT_sb, 1)

            def W_tile(s, k, mt, first):
                if not (first and k < WR):
                    act.wait_ge(e_used, (s - (WR - 1)) * H)
                nc.scalar.copy(Wt[:, k % WR, :, 0:WH],
                               W[:, bass.ds(mt, 1), :, :].rearrange("p t h w -> p (t h) w")).then_inc(Wt_ready, 1)

            def copy_sums(c, par, first):
                act.wait_ge(sums_done, c + 1)
                if not first:
                    act.wait_ge(out_stored, c * 16)
                nc.scalar.copy(sumT[:, :, :], psum[:, par * NB:(par + 1) * NB, :]).then_inc(sumT_ready, 1)

            def norm_stats(c, par):
                ln_junk = psum[:, par * NB:par * NB + 2, :].rearrange("p b (j f) -> p (b j) f", f=F)

                def done(ins, k):
                    ins.then_inc(act_step, 1)
                    act.wait_ge(act_step, c * 3 + k)

                act.wait_ge(z_ready, c + 1)
                for j in range(J):
                    last = nc.scalar.activation(ln_junk[:, j, :], z[:, j, :],
                                                ACT.Identity, accum_out=rsum[:, j:j + 1])
                done(last, 1)
                done(nc.scalar.mul(nmean[:, :], rsum[:, :], -1.0 / F), 2)
                for j in range(J):
                    last = nc.scalar.activation(ln_junk[:, j, :], z[:, j, :],
                                                ACT.Square, bias=nmean[:, j:j + 1], accum_out=ssq[:, j:j + 1])
                done(last, 3)
                nc.scalar.activation(std[:, :], ssq[:, :], ACT.Sqrt, bias=eps_t[:, 0:1], scale=1.0 / F).then_inc(std_ready, 1)

            def pair(c, gp, par, first=False, last=False, head=False, head_first=False):
                p = c * PAIRS + gp
                if first:
                    cast_unit(0, 1)
                    act.wait_ge(W_ready, 1)
                    act.wait_ge(Wt_zero, 1)
                for k in range(PS):
                    W_tile(p * PS + k, k, gp * PS + k, first)
                    if k % I == I - 1 and not last:
                        cast_unit(p + 1, k // I)
                    if k == 3 and head:
                        copy_sums(c - 1, 1 - par, head_first)
                if head:
                    norm_stats(c - 1, 1 - par)

            def chunk_tail(c, par):
                with act.Fori(1, PAIRS) as gp:
                    pair(c, gp, par)

            def two_chunks(cc, first=False):
                for par in range(2):
                    c = cc * 2 + par
                    chunk_tail(c, par)
                    pair(c + 1, 0, 1 - par, head=True, head_first=first and par == 0)

            pair(0, 0, 0, first=True)
            two_chunks(0, first=True)
            with act.Fori(1, CH // 2 - 1) as cc:
                two_chunks(cc)
            chunk_tail(CH - 2, 0)
            pair(CH - 1, 0, 1, head=True)
            with act.Fori(1, PAIRS - 1) as gp:
                pair(CH - 1, gp, 1)
            pair(CH - 1, PAIRS - 1, 1, last=True)
            copy_sums(CH - 1, 1, False)
            norm_stats(CH - 1, 1)

        @block.vector
        def _(dve):
            links = [0]

            def link(ins):
                links[0] += 1
                ins.then_inc(dve_step, 1)
                dve.wait_ge(dve_step, links[0])

            nc.vector.memset(zeros[:, :], 0.0).then_inc(consts, 1)
            nc.vector.memset(eps_t[:, :], EPS).then_inc(consts, 1)
            dve.wait_ge(ident_ok, 1)
            dve.wait_ge(w_loaded, 96)
            link(nc.vector.tensor_tensor(b_row[:, :], b_row[:, :], b2, ALU.add))
            for k in range(KT):
                for w in range(2):
                    link(nc.vector.tensor_tensor(wuv, Bs[:, k, 0:F], uv[:, w, :], ALU.mult))
                    ins = nc.vector.tensor_reduce(Bs[:, k, F + w * H:F + (w + 1) * H],
                                                  wuv.rearrange("p (h d) -> p h d", d=D), AX.X, ALU.add)
                    if k == KT - 1 and w == 1:
                        ins.then_inc(B_ready, 1)
                    else:
                        link(ins)
            dve.wait_ge(pwT_ready, 1)
            link(nc.vector.tensor_copy(PT[:, :, :], psum[:, 7, :].rearrange("p (k f) -> p k f", k=KT)))
            for k in range(KT):
                blk = PT[:, k, k * P:(k + 1) * P]
                nc.vector.tensor_tensor(blk, blk, ident[:, :], ALU.add).then_inc(PT_ready, 1)
            with dve.Fori(0, CH // 2) as gg:
                for b in range(2):
                    g = gg * 2 + b
                    dve.wait_ge(xT_psum, g + 1)
                    nc.vector.tensor_copy(xT[:, b, :, :], psum[:, 4:4 + KT, :]).then_inc(xT_sb, 1)
                    for j in range(J):
                        t = g * J + j
                        dve.wait_ge(Y_psum, t + 1)
                        nc.vector.tensor_tensor(Y[:, bass.ds(t, 1), :].rearrange("p t f -> p (t f)"),
                                                psum[:, 2 + j % 2, 0:F], b_row[:, :], ALU.add).then_inc(Y_out, 1)
            dve.wait_ge(S_out, 2 * MT)
            nc.vector.tensor_reduce(mx[:, :], f_all[:, 0:H, :], AX.X, ALU.max).then_inc(f1_max, 1)
            dve.wait_ge(c_ready, 1)
            link(nc.vector.tensor_scalar(nb_q[:, :], cmax[:, :], -(1 - NEG), K, ALU.mult, ALU.add))
            nc.vector.tensor_scalar(nb_c[:, :], cmax[:, :], -NEG, None, ALU.mult).then_inc(nb_ready, 1)
            nc.vector.tensor_scalar(f2zero[:, :, :], f_all[:, H:2 * H, :], 0.0, None, ALU.is_equal)
            for h in range(H):
                dve.wait_ge(C_ready, h + 1)
                Wh = W[:, :, h, 0:D]
                nc.vector.tensor_tensor(Wh, Wh, C[:, h, :].unsqueeze(2).to_broadcast([P, MT, D]), ALU.mult)
                nc.vector.tensor_copy(W[:, :, h, D], C[:, h, :])
                ins = nc.vector.scalar_tensor_tensor(W[:, :, h, D + 1], f_all[:, h, :], 0.0, C[:, h, :],
                                                     ALU.not_equal, ALU.mult)
            ins.then_inc(W_ready, 1)
            dve.wait_ge(q_ready, H)
            dve.wait_ge(Y_psum, MT)
            nc.vector.memset(Wt[:, :, :, WH:D + DT], 0.0).then_inc(Wt_zero, 1)

            def step(s, k, mt, b, first):
                i = k % I
                for h in range(H):
                    if not (first and k < EB // H):
                        dve.wait_ge(e_used, s * H + (h - EB + 1))
                    nc.vector.scalar_tensor_tensor(
                        e[:, (k * H + h) % EB, :].rearrange("p (j n) -> p j n", n=P),
                        r[:, b, h, :].rearrange("p (j n) -> p j n", n=P),
                        q[:, bass.ds(mt, 1), h],
                        adjT[:, k // I, :, i, :], ALU.max, ALU.mult).then_inc(e_ready, 1)

            def epilogue(c, par):
                dve.wait_ge(sums_psum, c + 1)
                n = [0]

                def small(ins):
                    n[0] += 1
                    ins.then_inc(dve_step, 1)
                    dve.wait_ge(dve_step, links[0] + c * 6 + n[0])

                both = bank(par, 2).rearrange("p (j h w) -> p j h w", j=J, h=H)
                z0 = f2zero[:, :, bass.ds(c * J, J)].rearrange("p h j -> p j h")
                small(nc.vector.tensor_copy(den[:, :, :], both[:, :, :, 0]))
                small(nc.vector.tensor_tensor(dif[:, :, :], both[:, :, :, 1], den[:, :, :], ALU.subtract))
                small(nc.vector.tensor_tensor(pos[:, :, :], dif[:, :, :], z0, ALU.mult))
                small(nc.vector.tensor_tensor(dif[:, :, :], den[:, :, :], pos[:, :, :], ALU.add))
                small(nc.vector.tensor_scalar(pos[:, :, :], dif[:, :, :], 1e-37, None, ALU.max))
                nc.vector.tensor_scalar(den[:, :, :], dif[:, :, :], 0.0, None, ALU.is_gt)
                small(nc.vector.reciprocal(rden[:, :, :], pos[:, :, :]))
                nc.vector.tensor_tensor(rden[:, :, :], rden[:, :, :], den[:, :, :], ALU.mult).then_inc(rden_ready, 1)
                dve.wait_ge(rden_ready, c + 1)
                for j in range(J):
                    for h in range(H):
                        y = Y[:, bass.ds(c * J + j, 1), h * D:(h + 1) * D].rearrange("p t f -> p (t f)")
                        num = bank(par, h // 2)[:, j * P + h % 2 * D:j * P + (h % 2 + 1) * D]
                        ins = nc.vector.scalar_tensor_tensor(z[:, j, h * D:(h + 1) * D], num,
                                                             rden[:, j, h:h + 1], y, ALU.mult, ALU.add)
                ins.then_inc(z_ready, 1)

            def normalise(c):
                dve.wait_ge(std_ready, c + 1)
                nc.vector.reciprocal(rstd[:, :], std[:, :]).then_inc(rstd_ready, 1)
                dve.wait_ge(rstd_ready, c + 1)
                nc.vector.tensor_tensor(nmr[:, :], nmean[:, :], rstd[:, :], ALU.mult).then_inc(nmr_ready, 1)
                dve.wait_ge(nmr_ready, c + 1)
                for j in range(J):
                    ins = nc.vector.tensor_scalar(z[:, j, :], z[:, j, :], rstd[:, j:j + 1], nmr[:, j:j + 1],
                                                  ALU.mult, ALU.add)
                ins.then_inc(out_ready, 1)

            def pair(c, gp, b, first=False, head=False):
                p = c * PAIRS + gp
                for k in range(PS):
                    if k % I == 0:
                        dve.wait_ge(adjT_loaded[k // I], p * 16 + 16)
                    step(p * PS + k, k, gp * PS + k, b, first)
                    if head and k == 4:
                        epilogue(c - 1, 1 - b)
                    if head and k == 7:
                        normalise(c - 1)

            def chunk_tail(c, b):
                with dve.Fori(1, PAIRS) as gp:
                    pair(c, gp, b)

            def two_chunks(cc):
                for par in range(2):
                    c = cc * 2 + par
                    chunk_tail(c, par)
                    dve.wait_ge(r_loaded[1 - par], cc * 16 + 16 * (1 + par))
                    pair(c + 1, 0, 1 - par, head=True)

            dve.wait_ge(r_loaded[0], 16)
            pair(0, 0, 0, first=True)
            two_chunks(0)
            with dve.Fori(1, CH // 2 - 1) as cc:
                two_chunks(cc)
            chunk_tail(CH - 2, 0)
            dve.wait_ge(r_loaded[1], 16 * (CH // 2))
            pair(CH - 1, 0, 1, head=True)
            chunk_tail(CH - 1, 1)
            epilogue(CH - 1, 1)
            normalise(CH - 1)

        @block.tensor
        def _(pe):
            pe.wait_ge(ident_ok, 1)
            pe.wait_ge(w_loaded, 96)
            for ki in range(KT):
                for ko in range(KT):
                    last = nc.tensor.transpose(psum[:, 7, ki * F + ko * P:ki * F + (ko + 1) * P],
                                               pw[:, ko, ki * P:(ki + 1) * P], ident[:, :])
            last.then_inc(pwT_ready, 1)
            pe.wait_ge(B_ready, 1)
            pe.wait_ge(PT_ready, KT)

            def x_transposes(g, b):
                for j in range(J):
                    for k in range(KT):
                        last = nc.tensor.transpose(psum[:, 4 + k, j * P:(j + 1) * P],
                                                   x_in[:, b, j, k * P:(k + 1) * P], ident[:, :])
                last.then_inc(xT_psum, 1)

            def products(g, b, first):
                pe.wait_ge(xT_sb, g + 1)
                for j in range(J):
                    t = g * J + j
                    if not (first and j < 2):
                        pe.wait_ge(S_out, (t - 1) * 2)
                    for k in range(KT):
                        last = nc.tensor.matmul(psum[:, j % 2, 0:F + 2 * H], xT[:, b, k, j * P:(j + 1) * P],
                                                Bs[:, k, :], start=(k == 0), stop=(k == KT - 1))
                    last.then_inc(S_psum, 1)
                    if not (first and j < 2):
                        pe.wait_ge(Y_out, t - 1)
                    for k in range(KT):
                        last = nc.tensor.matmul(psum[:, 2 + j % 2, 0:F], xT[:, b, k, j * P:(j + 1) * P],
                                                PT[:, k, :], start=(k == 0), stop=(k == KT - 1))
                    last.then_inc(Y_psum, 1)

            pe.wait_ge(x_loaded[0], 16)
            x_transposes(0, 0)
            products(0, 0, True)
            pe.wait_ge(x_loaded[1], 16)
            x_transposes(1, 1)
            products(1, 1, False)
            with pe.Fori(1, CH // 2) as gg:
                for b in range(2):
                    pe.wait_ge(x_loaded[b], gg * 16 + 16)
                    x_transposes(gg * 2 + b, b)
                    products(gg * 2 + b, b, False)
            pe.wait_ge(r_ready, H)
            for k in range(H * MT // P):
                last = nc.tensor.transpose(psum[:, 5, k * P:(k + 1) * P],
                                           r_nat.rearrange("p h t -> p (h t)")[:, k * P:(k + 1) * P], ident[:, :])
            last.then_inc(rT_psum, 1)

            def pair(c, gp, par, head=False, back=False):
                p = c * PAIRS + gp
                for k in range(PS):
                    s = p * PS + k
                    opens = head and k == 0
                    pe.wait_ge(Wt_ready, s + 1)
                    for h in range(H):
                        pe.wait_ge(e_ready, s * H + (h + 1))
                        nc.tensor.matmul(bank(par, h // 2)[h % 2 * D:(h % 2 + 1) * D, :], Wt[:, k % WR, h, 0:D],
                                         e[:, (k * H + h) % EB, :], start=opens, stop=False, skip_group_check=True)
                    for h in range(H):
                        nc.tensor.matmul(bank(par, 2)[h * DT:(h + 1) * DT, :], Wt[:, k % WR, h, D:D + DT],
                                         e[:, (k * H + h) % EB, :], start=opens, stop=False,
                                         skip_group_check=True).then_inc(e_used, 1)
                    if back and k == 1:
                        sums_back(c - 1, 1 - par)

            def chunk_end(par):
                for i in range(NB):
                    last = nc.tensor.matmul(bank(par, i), zeros[:, 0:P], zeros[:, :], start=False, stop=True,
                                            skip_group_check=True)
                last.then_inc(sums_done, 1)

            def sums_back(c, par):
                pe.wait_ge(sumT_ready, c + 1)
                for i in range(NB):
                    for j in range(J):
                        last = nc.tensor.transpose(bank(par, i)[:, j * P:(j + 1) * P],
                                                   sumT[:, i, j * P:(j + 1) * P], ident[:, :])
                last.then_inc(sums_psum, 1)

            def head_pair(c, par, first=False):
                if not first:
                    pe.wait_ge(out_ready, c - 1)
                pair(c, 0, par, head=True, back=True)

            def chunk_tail(c, par):
                with pe.Fori(1, PAIRS) as gp:
                    pair(c, gp, par)

            def two_chunks(cc, first=False):
                for par in range(2):
                    c = cc * 2 + par
                    chunk_tail(c, par)
                    chunk_end(par)
                    head_pair(c + 1, 1 - par, first and par == 0)

            pe.wait_ge(consts, 2)
            pe.wait_ge(S_out, 2 * MT)
            pe.wait_ge(Y_out, MT)
            pe.wait_ge(rT_sb, 1)
            pair(0, 0, 0, head=True)
            two_chunks(0, first=True)
            with pe.Fori(1, CH // 2 - 1) as cc:
                two_chunks(cc)
            chunk_tail(CH - 2, 0)
            chunk_end(0)
            head_pair(CH - 1, 1)
            chunk_tail(CH - 1, 1)
            chunk_end(1)
            sums_back(CH - 1, 1)


_INS = ["x", "adj", "L0_gnn_weight", "L0_gnn_weight_u", "L0_gnn_weight_v", "L0_gnn_bias", "L0_gnn_proj_w",
        "L0_gnn_proj_b"]


def kernel(**inputs):
    import numpy as _np
    import concourse.bacc as _bacc
    from concourse import mybir as _mybir
    from concourse.bass_utils import run_bass_kernel_spmd as _run

    nc = _bacc.Bacc("TRN2", target_bir_lowering=False, num_devices=1)
    arrays, args = {}, []
    for name in _INS:
        a = _np.ascontiguousarray(inputs[name])
        arrays[f"in_{name}"] = a
        args.append(nc.dram_tensor(f"in_{name}", a.shape, _mybir.dt.from_np(a.dtype), kind="ExternalInput").ap())
    out = nc.dram_tensor("out", inputs["x"].shape, _mybir.dt.float32, kind="ExternalOutput").ap()
    build(nc, *args, out)
    r = _run(nc, [arrays], core_ids=[0])
    return r.results[0]["out"]
```

```python
import math

import concourse.bass as bass
from concourse import mybir
from concourse.alu_op_type import AluOpType as ALU
from contextlib import ExitStack


def build(nc, x, adj, weight, weight_u, weight_v, bias, proj_w, proj_b, out):
    fp32, bf16, i32 = mybir.dt.float32, mybir.dt.bfloat16, mybir.dt.int32
    ACT = mybir.ActivationFunctionType
    AX = mybir.AxisListType
    RMAX = bass.bass_isa.ReduceOp.max

    P = 128
    N, F = x.shape
    H, D = weight_u.shape[0], weight_u.shape[1]
    KT = F // P
    MT = N // P
    NC = 512
    J = NC // P
    CH = N // NC
    WH = D + 2
    DT = 32
    WR = 4
    NB = 3
    UM = 512
    I = UM // P
    PAIRS = N // UM // 2
    PS = 2 * I
    SC = MT
    EB = 8
    K = 30.0
    R_MAX = math.exp(K + 1)
    EPS = 1e-5
    NEG = 0.2

    adj_v = adj.rearrange("(c j p) (g m) -> c g p j m", j=J, p=P, m=UM)
    x_v = x.rearrange("(g j p) f -> g p j f", j=J, p=P)
    out_v = out.rearrange("(c j p) f -> c p j f", j=J, p=P)

    ctx = ExitStack()
    with ctx:
        def sb(name, shape, dt):
            return ctx.enter_context(nc.sbuf_tensor(name, shape, dt))

        def sem(name):
            return ctx.enter_context(nc.semaphore(name))

        r_dram = nc.dram_tensor("r_rows", [H, N], fp32, kind="Internal").ap()

        W = sb("W", [P, MT, H, WH], fp32)
        Y = sb("Y", [P, MT, F], fp32)
        q = sb("q", [P, MT, H], fp32)
        f2zero = sb("f2zero", [P, H, MT], fp32)
        adj_raw = sb("adj_raw", [P, 2, J, UM], i32)
        adj_bf = sb("adj_bf", [P, J * UM], bf16)
        adjT = sb("adjT", [P, 2, J, I, P], bf16)
        e = sb("e", [P, EB, NC], fp32)
        r = sb("r", [P, 2, H, NC], fp32)
        sumT = sb("sumT", [P, NB, NC], fp32)
        z = sumT[:, 0:2, :].rearrange("p b (j f) -> p (b j) f", f=F)
        Wt = sb("Wt", [P, WR, H, D + DT], fp32)
        ident = sb("ident", [P, P], fp32)
        eps_t = sb("eps_t", [P, 1], fp32)
        mx = sb("mx", [P, H], fp32)
        cmax = sb("cmax", [P, H], fp32)
        nb_q = sb("nb_q", [P, H], fp32)
        nb_c = sb("nb_c", [P, H], fp32)
        rsum = sb("rsum", [P, J], fp32)
        nmean = sb("nmean", [P, J], fp32)
        ssq = sb("ssq", [P, J], fp32)
        std = sb("std", [P, J], fp32)
        rstd = sb("rstd", [P, J], fp32)
        nmr = sb("nmr", [P, J], fp32)
        den = sb("den", [P, J, H], fp32)
        dif = sb("dif", [P, J, H], fp32)
        pos = sb("pos", [P, J, H], fp32)
        rden = sb("rden", [P, J, H], fp32)
        x_in = e[:, 0:4, :].rearrange("p (b j) c -> p b (j c)", b=2).rearrange("p b (j f) -> p b j f", f=F)
        xT = e[:, 4:8, :].rearrange("p (b k) n -> p b k n", b=2)
        r1 = r[:, 1, :, :].rearrange("p h n -> p (h n)")
        uv = r1[:, 0:2 * F].rearrange("p (w f) -> p w f", w=2)
        wuv = r1[:, 512:512 + F]
        f_all = r1[:, 768:768 + 2 * H * MT].rearrange("p (h t) -> p h t", t=MT)
        r_nat = r1[:, 1280:1280 + H * MT].rearrange("p (h t) -> p h t", t=MT)
        r_T = r1[:, 1536:1536 + H * MT].rearrange("p (k n) -> p k n", n=P)
        b2 = sumT[:, 0, 0:F]
        b_row = sumT[:, 0, F:2 * F]
        pw = sumT[:, 1, :].rearrange("p (k f) -> p k f", k=KT)
        Wt_flat = Wt[:, :, :, :].rearrange("p r h w -> p (r h w)")
        BW = F + 2 * H
        Bs = Wt_flat[:, 0:KT * BW].rearrange("p (k c) -> p k c", k=KT)
        PT = Wt_flat[:, KT * BW:KT * (BW + F)].rearrange("p (k c) -> p k c", k=KT)
        psum = ctx.enter_context(nc.psum_tensor("psum", [P, 8, 512], fp32))
        def bank(par, i):
            return psum[:, par * NB + i, :]


        x_loaded = [sem(f"x_loaded{b}") for b in range(2)]
        B_loaded = sem("B_loaded")
        w_loaded = sem("w_loaded")
        eps_ready = sem("eps_ready")
        ident_z = sem("ident_z")
        ident_ok = sem("ident_ok")
        dve_step = sem("dve_step")
        B_ready = sem("B_ready")
        pwT_ready = sem("pwT_ready")
        PT_ready = sem("PT_ready")
        xT_psum = sem("xT_psum")
        xT_sb = sem("xT_sb")
        S_psum = sem("S_psum")
        Y_psum = sem("Y_psum")
        S_out = sem("S_out")
        Y_out = sem("Y_out")
        f1_max = sem("f1_max")
        c_ready = sem("c_ready")
        nb_ready = sem("nb_ready")
        C_ready = sem("C_ready")
        q_ready = sem("q_ready")
        r_ready = sem("r_ready")
        r_bounded = sem("r_bounded")
        rT_psum = sem("rT_psum")
        r0_psum = sem("r0_psum")
        r0_ready = sem("r0_ready")
        rT_sb = sem("rT_sb")
        r_stored = sem("r_stored")
        W_ready = sem("W_ready")
        r_loaded = [sem(f"r_loaded{b}") for b in range(2)]
        adj_loaded = [sem(f"adj_loaded{b}") for b in range(2)]
        adj_cast = sem("adj_cast")
        adjT_loaded = [sem(f"adjT_loaded{b}") for b in range(2)]
        e_ready = sem("e_ready")
        e_used = sem("e_used")
        Wt_ready = sem("Wt_ready")
        Wt_zero = sem("Wt_zero")
        sumT_ready = sem("sumT_ready")
        sums_psum = sem("sums_psum")
        z_ready = sem("z_ready")
        act_step = sem("act_step")
        std_ready = sem("std_ready")
        rstd_ready = sem("rstd_ready")
        nmr_ready = sem("nmr_ready")
        den_part = sem("den_part")
        attn_ready = sem("attn_ready")
        out_ready = sem("out_ready")
        out_stored = sem("out_stored")

        block = ctx.enter_context(nc.Block())

        @block.sync
        def _(sp):
            sp.dma_start(Bs[:, :, 0:F], weight.rearrange("(k p) c -> p k c", p=P)).then_inc(B_loaded, 16)
            sp.dma_start(uv[:, 0, :], weight_u.rearrange("h d o -> (o h d)").partition_broadcast(P)).then_inc(B_loaded, 16)
            sp.dma_start(uv[:, 1, :], weight_v.rearrange("h d o -> (o h d)").partition_broadcast(P)).then_inc(B_loaded, 16)
            sp.dma_start(pw, proj_w.rearrange("(k p) c -> p k c", p=P)).then_inc(w_loaded, 16)
            sp.dma_start(x_in[:, 0, :, :], x_v[0]).then_inc(x_loaded[0], 16)
            sp.dma_start(b_row[:, :], bias[0, :].partition_broadcast(P)).then_inc(w_loaded, 16)
            sp.dma_start(b2, proj_b.partition_broadcast(P)).then_inc(w_loaded, 16)
            sp.dma_start(x_in[:, 1, :, :], x_v[1]).then_inc(x_loaded[1], 16)

            def load_unit(c, g, b):
                sp.dma_start(adj_raw[:, b, :, :], adj_v[c, g]).then_inc(adj_loaded[b], 16)

            def transpose_unit(b):
                sp.dma_start(adjT[:, b, :, :, :].rearrange("p j i n -> p (j i) n"), adj_bf[:, :],
                             transpose=True).then_inc(adjT_loaded[b], 16)

            load_unit(0, 0, 0)
            load_unit(0, 1, 1)
            with sp.Fori(1, CH // 2) as gg:
                for b in range(2):
                    sp.wait_ge(xT_psum, gg * 2 + (b - 1))
                    sp.dma_start(x_in[:, b, :, :], x_v[gg * 2 + b]).then_inc(x_loaded[b], 16)
            sp.wait_ge(adj_cast, 1)
            transpose_unit(0)
            sp.wait_ge(rT_sb, 1)
            sp.dma_start(r_dram.rearrange("h (t p) -> (h t) p", p=P).rearrange("(k q) p -> q k p", q=P),
                         r_T).then_inc(r_stored, 16)
            sp.wait_ge(r_stored, 16)

            def load_r(c, b):
                src = r_dram.rearrange("h (c n) -> c h n", n=NC)[c].partition_broadcast(P)
                sp.dma_start(r[:, b, :, :], src).then_inc(r_loaded[b], 16)

            def first_units():
                for b in range(2):
                    sp.wait_ge(adj_cast, 2 + b)
                    if b:
                        sp.wait_ge(e_ready, I * H)
                    load_unit(0, 2 + b, b)
                    transpose_unit(1 - b)

            def load_pair(c, gp):
                u = (c * PAIRS + gp) * 2
                for b in range(2):
                    sp.wait_ge(adj_cast, u + b)
                    sp.wait_ge(e_ready, (u + (b - 2)) * (I * H))
                    load_unit(c, gp * 2 + b, b)
                    transpose_unit(1 - b)

            def chunk_tail(c):
                with sp.Fori(1, PAIRS) as gp:
                    load_pair(c, gp)

            def next_r(c, b, first=False):
                if first:
                    sp.wait_ge(W_ready, 1)
                    sp.wait_ge(C_ready, H)
                    sp.wait_ge(r0_psum, 1)
                else:
                    sp.wait_ge(e_ready, c * (SC * H))
                load_r(c + 1, b)

            def two_chunks(cc):
                for par in range(2):
                    c = cc * 2 + par
                    chunk_tail(c)
                    next_r(c, 1 - par)
                    load_pair(c + 1, 0)

            first_units()
            with sp.Fori(2, PAIRS) as gp:
                load_pair(0, gp)
            next_r(0, 1, first=True)
            load_pair(1, 0)
            chunk_tail(1)
            next_r(1, 0)
            load_pair(2, 0)
            with sp.Fori(1, CH // 2 - 1) as cc:
                two_chunks(cc)
            chunk_tail(CH - 2)
            next_r(CH - 2, 1)
            load_pair(CH - 1, 0)
            chunk_tail(CH - 1)
            sp.wait_ge(adj_cast, CH * PAIRS * 2)
            sp.wait_ge(e_ready, (CH * PAIRS * 2 - 2) * (I * H))
            transpose_unit(1)

        @block.gpsimd
        def _(pool):
            nc.gpsimd.memset(ident[:, :], 0.0).then_inc(ident_z, 1)
            pool.wait_ge(ident_z, 1)
            nc.gpsimd.affine_select(out=ident[:, :], in_=ident[:, :], compare_op=ALU.not_equal, fill=1.0,
                                    base=0, pattern=[[-1, P]], channel_multiplier=1).then_inc(ident_ok, 1)
            pool.wait_ge(f1_max, 1)
            nc.gpsimd.partition_all_reduce(cmax[:, :], mx[:, :], P, RMAX).then_inc(c_ready, 1)
            with pool.Fori(0, CH) as c:
                pool.wait_ge(out_ready, c + 1)
                pool.dma_start(out_v[c], z[:, :, :]).then_inc(out_stored, 16)
            pool.wait_ge(out_stored, 16 * CH)

        @block.scalar
        def _(act):
            def cast_unit(pair, b, first=False):
                act.wait_ge(adj_loaded[b], pair * 16 + 16)
                if not (first and b == 0):
                    act.wait_ge(adjT_loaded[1 - b], (pair + b) * 16)
                nc.scalar.copy(adj_bf[:, :], adj_raw[:, b, :, :].rearrange("p j m -> p (j m)")).then_inc(adj_cast, 1)

            act.wait_ge(xT_psum, 1)
            nc.scalar.copy(xT[:, 0, :, :], psum[:, 4:4 + KT, :]).then_inc(xT_sb, 1)
            with act.Fori(0, CH) as g:
                for j in range(J):
                    act.wait_ge(S_psum, g * J + (j + 1))
                    nc.scalar.copy(W[:, bass.ds(g * J + j, 1), :, 0:D].rearrange("p t h d -> p (t h) d"),
                                   psum[:, j % 2, 0:F].rearrange("p (h d) -> p h d", d=D)).then_inc(S_out, 1)
                    nc.scalar.copy(f_all[:, :, bass.ds(g * J + j, 1)].rearrange("p h t -> p (h t)"),
                                   psum[:, j % 2, F:F + 2 * H]).then_inc(S_out, 1)
            cast_unit(0, 0, first=True)
            act.wait_ge(eps_ready, 1)
            act.wait_ge(nb_ready, 1)
            for h in range(H):
                nc.scalar.activation(r_nat[:, h, :], f_all[:, H + h, :], ACT.Exp, bias=nb_q[:, h:h + 1],
                                     scale=-(1 - NEG)).then_inc(r_ready, 1)
            for h in range(H):
                nc.scalar.activation(q[:, :, h], f_all[:, h, :], ACT.Exp, bias=nb_q[:, h:h + 1],
                                     scale=1 - NEG).then_inc(q_ready, 1)
            for h in range(H):
                nc.scalar.activation(W[:, :, h, D], f_all[:, h, :], ACT.Exp, bias=nb_c[:, h:h + 1],
                                     scale=NEG).then_inc(C_ready, 1)
            act.wait_ge(r0_psum, 1)
            for h in range(H):
                nc.scalar.copy(r[:, 0, h, :], psum[:, h, :]).then_inc(r0_ready, 1)

            def copy_rT():
                act.wait_ge(rT_psum, 1)
                nc.scalar.copy(r_T, psum[:, 5, 0:H * MT].rearrange("p (k n) -> p k n", n=P)).then_inc(rT_sb, 1)

            def W_tile(s, k, mt, first):
                if not (first and k < WR):
                    act.wait_ge(e_used, (s - (WR - 1)) * H)
                nc.scalar.copy(Wt[:, k % WR, :, D:WH],
                               W[:, bass.ds(mt, 1), :, D:WH].rearrange("p t h w -> p (t h) w")).then_inc(Wt_ready, 1)
                for h in range(H):
                    nc.scalar.activation(Wt[:, k % WR, h, 0:D], W[:, bass.ds(mt, 1), h, 0:D].rearrange("p t d -> p (t d)"),
                                         ACT.Copy, scale=W[:, bass.ds(mt, 1), h, D]).then_inc(Wt_ready, 1)

            def copy_sums(c, par, first):
                act.wait_ge(e_used, (c + 1) * (SC * H))
                if not first:
                    act.wait_ge(out_stored, c * 16)
                nc.scalar.copy(sumT[:, :, :], psum[:, par * NB:(par + 1) * NB, :]).then_inc(sumT_ready, 1)

            def attend(c, par):
                act.wait_ge(den_part, c * 8 + 8)
                for j in range(J):
                    for h in range(H):
                        num = bank(par, h // 2)[:, j * P + h % 2 * D:j * P + (h % 2 + 1) * D]
                        ins = nc.scalar.activation(z[:, j, h * D:(h + 1) * D], num, ACT.Copy,
                                                   scale=rden[:, j, h:h + 1])
                ins.then_inc(attn_ready, 1)

            def norm_stats(c, par):
                ln_junk = psum[:, par * NB:par * NB + 2, :].rearrange("p b (j f) -> p (b j) f", f=F)

                def done(ins, k):
                    ins.then_inc(act_step, 1)
                    act.wait_ge(act_step, c * 3 + k)

                for j in range(J):
                    act.wait_ge(z_ready, c * J + (j + 1))
                    last = nc.scalar.activation(ln_junk[:, j, :], z[:, j, :],
                                                ACT.Identity, accum_out=rsum[:, j:j + 1])
                done(last, 1)
                done(nc.scalar.mul(nmean[:, :], rsum[:, :], -1.0 / F), 2)
                for j in range(J):
                    last = nc.scalar.activation(ln_junk[:, j, :], z[:, j, :],
                                                ACT.Square, bias=nmean[:, j:j + 1], accum_out=ssq[:, j:j + 1])
                done(last, 3)
                nc.scalar.activation(std[:, :], ssq[:, :], ACT.Sqrt, bias=eps_t[:, 0:1], scale=1.0 / F).then_inc(std_ready, 1)

            def normalise(c):
                act.wait_ge(nmr_ready, c + 1)
                for j in range(J):
                    ins = nc.scalar.activation(z[:, j, :], z[:, j, :], ACT.Identity, bias=nmr[:, j:j + 1],
                                               scale=rstd[:, j:j + 1])
                ins.then_inc(out_ready, 1)

            def pair(c, gp, par, first=False, last=False, ending=False, ending_first=False):
                p = c * PAIRS + gp
                if first:
                    act.wait_ge(W_ready, 1)
                    act.wait_ge(Wt_zero, 1)
                for k in range(PS):
                    W_tile(p * PS + k, k, gp * PS + k, first)
                    if first and k == 1:
                        cast_unit(0, 1)
                    if first and k == 2:
                        copy_rT()
                    if ending and (gp, k) == (0, 3):
                        copy_sums(c - 1, 1 - par, ending_first)
                    if k % I == I - 1 and not last:
                        cast_unit(p + 1, k // I)
                    if ending and (gp, k) == (1, 0):
                        attend(c - 1, 1 - par)
                    if ending and (gp, k) == (1, 5):
                        norm_stats(c - 1, 1 - par)
                if ending and gp == 1:
                    normalise(c - 1)

            def chunk_head(c, par, ending_first=False):
                pair(c, 0, par, ending=True, ending_first=ending_first)
                pair(c, 1, par, ending=True)

            def chunk_tail(c, par):
                with act.Fori(2, PAIRS) as gp:
                    pair(c, gp, par)

            def two_chunks(cc, first=False):
                for par in range(2):
                    c = cc * 2 + par
                    chunk_tail(c, par)
                    chunk_head(c + 1, 1 - par, first and par == 0)

            pair(0, 0, 0, first=True)
            pair(0, 1, 0)
            two_chunks(0, first=True)
            with act.Fori(1, CH // 2 - 1) as cc:
                two_chunks(cc)
            chunk_tail(CH - 2, 0)
            chunk_head(CH - 1, 1)
            with act.Fori(2, PAIRS - 1) as gp:
                pair(CH - 1, gp, 1)
            pair(CH - 1, PAIRS - 1, 1, last=True)
            copy_sums(CH - 1, 1, False)
            attend(CH - 1, 1)
            norm_stats(CH - 1, 1)
            normalise(CH - 1)

        @block.vector
        def _(dve):
            links = [0]

            def link(ins):
                links[0] += 1
                ins.then_inc(dve_step, 1)
                dve.wait_ge(dve_step, links[0])

            nc.vector.memset(eps_t[:, :], EPS).then_inc(eps_ready, 1)
            dve.wait_ge(ident_ok, 1)
            dve.wait_ge(B_loaded, 48)
            for k in range(KT):
                for w in range(2):
                    link(nc.vector.tensor_tensor(wuv, Bs[:, k, 0:F], uv[:, w, :], ALU.mult))
                    ins = nc.vector.tensor_reduce(Bs[:, k, F + w * H:F + (w + 1) * H],
                                                  wuv.rearrange("p (h d) -> p h d", d=D), AX.X, ALU.add)
                    if k == KT - 1 and w == 1:
                        ins.then_inc(B_ready, 1)
                    else:
                        link(ins)
            dve.wait_ge(w_loaded, 48)
            link(nc.vector.tensor_tensor(b_row[:, :], b_row[:, :], b2, ALU.add))
            dve.wait_ge(pwT_ready, 1)
            link(nc.vector.tensor_copy(PT[:, :, :], psum[:, 7, :].rearrange("p (k f) -> p k f", k=KT)))
            for k in range(KT):
                blk = PT[:, k, k * P:(k + 1) * P]
                nc.vector.tensor_tensor(blk, blk, ident[:, :], ALU.add).then_inc(PT_ready, 1)
            def copy_xT(g, b):
                dve.wait_ge(xT_psum, g + 1)
                nc.vector.tensor_copy(xT[:, b, :, :], psum[:, 4:4 + KT, :]).then_inc(xT_sb, 1)

            def Y_tiles(g, b, last=False):
                for j in range(J):
                    t = g * J + j
                    dve.wait_ge(Y_psum, t + 1)
                    nc.vector.tensor_tensor(Y[:, bass.ds(t, 1), :].rearrange("p t f -> p (t f)"),
                                            psum[:, 2 + j % 2, 0:F], b_row[:, :], ALU.add).then_inc(Y_out, 1)
                    if j == 0 and not last:
                        copy_xT(g + 1, 1 - b)

            with dve.Fori(0, CH // 2 - 1) as gg:
                for b in range(2):
                    Y_tiles(gg * 2 + b, b)
            Y_tiles(CH - 2, 0)
            Y_tiles(CH - 1, 1, last=True)
            dve.wait_ge(S_out, 2 * MT)
            nc.vector.tensor_reduce(mx[:, :], f_all[:, 0:H, :], AX.X, ALU.max).then_inc(f1_max, 1)
            dve.wait_ge(c_ready, 1)
            link(nc.vector.tensor_scalar(nb_q[:, :], cmax[:, :], -(1 - NEG), K, ALU.mult, ALU.add))
            nc.vector.tensor_scalar(nb_c[:, :], cmax[:, :], -NEG, None, ALU.mult).then_inc(nb_ready, 1)
            dve.wait_ge(r_ready, H)
            nc.vector.tensor_scalar(r_nat, r_nat, R_MAX, None, ALU.min).then_inc(r_bounded, 1)
            nc.vector.tensor_scalar(f2zero[:, :, :], f_all[:, H:2 * H, :], 0.0, None, ALU.is_equal)
            for h in range(H):
                dve.wait_ge(C_ready, h + 1)
                ins = nc.vector.scalar_tensor_tensor(W[:, :, h, D + 1], f_all[:, h, :], 0.0, W[:, :, h, D],
                                                     ALU.not_equal, ALU.mult)
            ins.then_inc(W_ready, 1)
            dve.wait_ge(q_ready, H)
            dve.wait_ge(Y_psum, MT)
            nc.vector.memset(Wt[:, :, :, WH:D + DT], 0.0).then_inc(Wt_zero, 1)

            def denominator_part(i, c, par):
                both = bank(par, 2).rearrange("p (j h w) -> p j h w", j=J, h=H)
                z0 = f2zero[:, :, bass.ds(c * J, J)].rearrange("p h j -> p j h")
                if i == 0:
                    dve.wait_ge(sums_psum, c + 1)
                    ins = nc.vector.tensor_copy(den[:, :, :], both[:, :, :, 0])
                else:
                    dve.wait_ge(den_part, c * 8 + i)
                if i == 1:
                    ins = nc.vector.tensor_tensor(dif[:, :, :], both[:, :, :, 1], den[:, :, :], ALU.subtract)
                if i == 2:
                    ins = nc.vector.tensor_tensor(pos[:, :, :], dif[:, :, :], z0, ALU.mult)
                if i == 3:
                    ins = nc.vector.tensor_tensor(dif[:, :, :], den[:, :, :], pos[:, :, :], ALU.add)
                if i == 4:
                    ins = nc.vector.tensor_scalar(pos[:, :, :], dif[:, :, :], 1e-37, None, ALU.max)
                if i == 5:
                    ins = nc.vector.tensor_scalar(den[:, :, :], dif[:, :, :], 0.0, None, ALU.is_gt)
                if i == 6:
                    ins = nc.vector.reciprocal(dif[:, :, :], pos[:, :, :])
                if i == 7:
                    ins = nc.vector.tensor_tensor(rden[:, :, :], dif[:, :, :], den[:, :, :], ALU.mult)
                ins.then_inc(den_part, 1)

            def add_Y(j, c):
                if j == 0:
                    dve.wait_ge(attn_ready, c + 1)
                nc.vector.tensor_tensor(z[:, j, :], z[:, j, :], Y[:, bass.ds(c * J + j, 1), :].rearrange("p t f -> p (t f)"),
                                        ALU.add).then_inc(z_ready, 1)

            def rstd_part(i, c):
                if i == 0:
                    dve.wait_ge(std_ready, c + 1)
                    nc.vector.reciprocal(rstd[:, :], std[:, :]).then_inc(rstd_ready, 1)
                if i == 1:
                    dve.wait_ge(rstd_ready, c + 1)
                    nc.vector.tensor_tensor(nmr[:, :], nmean[:, :], rstd[:, :], ALU.mult).then_inc(nmr_ready, 1)

            def pair(c, gp, b, first=False, ending=False):
                p = c * PAIRS + gp
                for k in range(PS):
                    if k % I == 0:
                        dve.wait_ge(adjT_loaded[k // I], p * 16 + 16)
                    for h in range(H):
                        score(p * PS + k, k, gp * PS + k, h, b, first)
                        if ending and gp == 0 and k >= 4 and h % 2 == 0:
                            denominator_part((k - 4) * 2 + h // 2, c - 1, 1 - b)
                        if ending and gp == 1 and 1 <= k < 1 + J and h == 0:
                            add_Y(k - 1, c - 1)
                        if ending and gp == 1 and k == PS - 2 and h >= 2:
                            rstd_part(h - 2, c - 1)

            def score(s, k, mt, h, b, first):
                if first and k == 0:
                    dve.wait_ge(r0_ready, h + 1)
                if not (first and k < EB // H):
                    dve.wait_ge(e_used, s * H + (h - EB + 1))
                nc.vector.scalar_tensor_tensor(
                    e[:, (k * H + h) % EB, :].rearrange("p (j n) -> p j n", n=P),
                    r[:, b, h, :].rearrange("p (j n) -> p j n", n=P),
                    q[:, bass.ds(mt, 1), h],
                    adjT[:, k // I, :, k % I, :], ALU.max, ALU.mult).then_inc(e_ready, 1)

            def chunk_head(c, b):
                pair(c, 0, b, ending=True)
                pair(c, 1, b, ending=True)

            def chunk_tail(c, b):
                with dve.Fori(2, PAIRS) as gp:
                    pair(c, gp, b)

            def two_chunks(cc):
                for par in range(2):
                    c = cc * 2 + par
                    chunk_tail(c, par)
                    dve.wait_ge(r_loaded[1 - par], cc * 16 + 16)
                    chunk_head(c + 1, 1 - par)

            pair(0, 0, 0, first=True)
            pair(0, 1, 0)
            two_chunks(0)
            with dve.Fori(1, CH // 2 - 1) as cc:
                two_chunks(cc)
            chunk_tail(CH - 2, 0)
            dve.wait_ge(r_loaded[1], 16 * (CH // 2))
            chunk_head(CH - 1, 1)
            chunk_tail(CH - 1, 1)
            for i in range(8):
                denominator_part(i, CH - 1, 1)
            for j in range(J):
                add_Y(j, CH - 1)
            for i in range(2):
                rstd_part(i, CH - 1)

        @block.tensor
        def _(pe):
            def x_transposes(g, b):
                for j in range(J):
                    for k in range(KT):
                        last = nc.tensor.transpose(psum[:, 4 + k, j * P:(j + 1) * P],
                                                   x_in[:, b, j, k * P:(k + 1) * P], ident[:, :])
                last.then_inc(xT_psum, 1)

            pe.wait_ge(ident_ok, 1)
            pe.wait_ge(x_loaded[0], 16)
            x_transposes(0, 0)
            pe.wait_ge(w_loaded, 48)
            for ki in range(KT):
                for ko in range(KT):
                    last = nc.tensor.transpose(psum[:, 7, ki * F + ko * P:ki * F + (ko + 1) * P],
                                               pw[:, ko, ki * P:(ki + 1) * P], ident[:, :])
            last.then_inc(pwT_ready, 1)
            pe.wait_ge(B_ready, 1)
            pe.wait_ge(PT_ready, KT)

            def products(g, b, first=False, last=False):
                pe.wait_ge(xT_sb, g + 1)
                for j in range(J):
                    t = g * J + j
                    if not (first and j < 2):
                        pe.wait_ge(S_out, (t - 1) * 2)
                    for k in range(KT):
                        ins = nc.tensor.matmul(psum[:, j % 2, 0:F + 2 * H], xT[:, b, k, j * P:(j + 1) * P],
                                               Bs[:, k, :], start=(k == 0), stop=(k == KT - 1))
                    ins.then_inc(S_psum, 1)
                    if not (first and j < 2):
                        pe.wait_ge(Y_out, t - 1)
                    for k in range(KT):
                        ins = nc.tensor.matmul(psum[:, 2 + j % 2, 0:F], xT[:, b, k, j * P:(j + 1) * P],
                                               PT[:, k, :], start=(k == 0), stop=(k == KT - 1))
                    ins.then_inc(Y_psum, 1)
                    if j == 0 and not last:
                        pe.wait_ge(x_loaded[1 - b], (g + b) * 8 + 16)
                        x_transposes(g + 1, 1 - b)

            products(0, 0, first=True)
            products(1, 1)
            with pe.Fori(1, CH // 2 - 1) as gg:
                for b in range(2):
                    products(gg * 2 + b, b)
            products(CH - 2, 0)
            products(CH - 1, 1, last=True)
            pe.wait_ge(S_out, 2 * MT)
            pe.wait_ge(Y_out, MT)
            pe.wait_ge(r_bounded, 1)
            for h in range(H):
                for j in range(J):
                    ins = nc.tensor.transpose(psum[:, h, j * P:(j + 1) * P],
                                              r_nat[:, h, j:j + 1].to_broadcast([P, P]), ident[:, :])
            ins.then_inc(r0_psum, 1)
            for k in range(H * MT // P):
                last = nc.tensor.transpose(psum[:, 5, k * P:(k + 1) * P],
                                           r_nat.rearrange("p h t -> p (h t)")[:, k * P:(k + 1) * P], ident[:, :])
            last.then_inc(rT_psum, 1)

            def numerator(k, h, par, opens, closes):
                return nc.tensor.matmul(bank(par, h // 2)[h % 2 * D:(h % 2 + 1) * D, :], Wt[:, k % WR, h, 0:D],
                                        e[:, (k * H + h) % EB, :], start=opens, stop=closes, skip_group_check=True)

            def denominator(k, h, par, opens, closes):
                return nc.tensor.matmul(bank(par, 2)[h * DT:(h + 1) * DT, :], Wt[:, k % WR, h, D:D + DT],
                                        e[:, (k * H + h) % EB, :], start=opens, stop=closes, skip_group_check=True)

            def pair(c, gp, par, head=False, back=False, last=False):
                p = c * PAIRS + gp
                for k in range(PS):
                    s = p * PS + k
                    opens = head and k == 0
                    closes = last and k == PS - 1
                    pe.wait_ge(Wt_ready, (s + 1) * (H + 1))
                    for h in range(H):
                        pe.wait_ge(e_ready, s * H + (h + 1))
                        numerator(k, h, par, opens, closes)
                    for h in range(H):
                        denominator(k, h, par, opens, closes).then_inc(e_used, 1)
                    if back and k == 2:
                        sums_back(c - 1, 1 - par)

            def sums_back(c, par):
                pe.wait_ge(sumT_ready, c + 1)
                for i in range(NB):
                    for j in range(J):
                        last = nc.tensor.transpose(bank(par, i)[:, j * P:(j + 1) * P],
                                                   sumT[:, i, j * P:(j + 1) * P], ident[:, :])
                last.then_inc(sums_psum, 1)

            def head_pair(c, par, first=False):
                if first:
                    pe.wait_ge(rT_sb, 1)
                else:
                    pe.wait_ge(out_ready, c - 1)
                pair(c, 0, par, head=True, back=True)

            def chunk_tail(c, par):
                with pe.Fori(1, PAIRS - 1) as gp:
                    pair(c, gp, par)
                pair(c, PAIRS - 1, par, last=True)

            def two_chunks(cc, first=False):
                for par in range(2):
                    c = cc * 2 + par
                    chunk_tail(c, par)
                    head_pair(c + 1, 1 - par, first and par == 0)

            pe.wait_ge(r0_ready, H)
            pair(0, 0, 0, head=True)
            two_chunks(0, first=True)
            with pe.Fori(1, CH // 2 - 1) as cc:
                two_chunks(cc)
            chunk_tail(CH - 2, 0)
            head_pair(CH - 1, 1)
            chunk_tail(CH - 1, 1)
            sums_back(CH - 1, 1)


_INS = ["x", "adj", "L0_gnn_weight", "L0_gnn_weight_u", "L0_gnn_weight_v", "L0_gnn_bias", "L0_gnn_proj_w",
        "L0_gnn_proj_b"]


def kernel(**inputs):
    import numpy as _np
    import concourse.bacc as _bacc
    from concourse import mybir as _mybir
    from concourse.bass_utils import run_bass_kernel_spmd as _run

    nc = _bacc.Bacc("TRN2", target_bir_lowering=False, num_devices=1)
    arrays, args = {}, []
    for name in _INS:
        a = _np.ascontiguousarray(inputs[name])
        arrays[f"in_{name}"] = a
        args.append(nc.dram_tensor(f"in_{name}", a.shape, _mybir.dt.from_np(a.dtype), kind="ExternalInput").ap())
    out = nc.dram_tensor("out", inputs["x"].shape, _mybir.dt.float32, kind="ExternalOutput").ap()
    build(nc, *args, out)
    r = _run(nc, [arrays], core_ids=[0])
    return r.results[0]["out"]
```
